# Optimizing a Trainium2 kernel written in Bass

```python
import numpy as np
import jax
import jax.numpy as jnp

def _softmax(x, axis=-1):
    return jax.nn.softmax(x, axis=axis)

def _gelu(x):
    return jax.nn.gelu(x, approximate=True)

def _silu(x):
    return jax.nn.silu(x)

def _sigmoid(x):
    return jax.nn.sigmoid(x)

def _layernorm(x, axis=-1, eps=1e-05):
    m = jnp.mean(x, axis=axis, keepdims=True)
    v = jnp.var(x, axis=axis, keepdims=True)
    return (x - m) / jnp.sqrt(v + eps)

def _scatter_add(tgt, idx, src, axis=0):
    return tgt.at[idx].add(src)

def _segment_sum(src, seg, n):
    return jax.ops.segment_sum(src, seg, n)
kernel_name = 'mk_xattn_seq_d2_seqx_r4_0fff61'

def setup_inputs(seed: int=0):
    np.random.seed(seed)
    _w = jnp.asarray

    def _rec_inputs():
        import jax
        import jax.numpy as jnp
        _rk = jax.random.key(seed)
        x = -0.000125 + 0.9999 * jax.random.normal(jax.random.fold_in(_rk, 1), (16, 256, 512), jnp.float32)
        _lenS = 256 - jax.random.randint(jax.random.fold_in(_rk, 7), (16,), 0, max(1, 256 // 4) + 1, jnp.int32)
        _lenS2 = 256 - jax.random.randint(jax.random.fold_in(_rk, 8), (16,), 0, max(1, 256 // 4) + 1, jnp.int32)
        _ctx_2048P = jax.random.normal(jax.random.fold_in(_rk, 11), (16, 16, 512), jnp.float32)
        _ctx_2048c = jax.random.dirichlet(jax.random.fold_in(_rk, 511), 0.3 * jnp.ones((16,), jnp.float32), (16, 256))
        _ctx_2048t = jnp.einsum('bsk,bkd->bsd', _ctx_2048c, _ctx_2048P)
        _ctx_2048t = _ctx_2048t * jax.lax.rsqrt(jnp.mean(jnp.square(_ctx_2048t)) + 1e-12) * 0.953939
        ctx_2048 = -0.00401388 + 1.00018 * (_ctx_2048t + 0.3 * jax.random.normal(jax.random.fold_in(_rk, 611), (16, 256, 512), jnp.float32))
        return (x, ctx_2048)
    x, ctx_2048 = _rec_inputs()

    def _L0_xattn_setup():
        import jax, jax.numpy as jnp
        import numpy as np
        H = 512
        B, L, S = (4, 1024, 10)
        key = jax.random.key(seed)
        k1, k2, k3, k4, k5, k6 = jax.random.split(key, 6)
        scale = 1.0 / np.sqrt(H)
        return {'h_english': jax.random.normal(k1, (B, L, H), dtype=jnp.float32), 'h_lojban': jax.random.normal(k2, (B, S, H), dtype=jnp.float32), 'w_q': jax.random.normal(k3, (H, H), dtype=jnp.float32) * scale, 'w_k': jax.random.normal(k4, (H, H), dtype=jnp.float32) * scale, 'w_v': jax.random.normal(k5, (H, H), dtype=jnp.float32) * scale, 'w_o': jax.random.normal(k6, (H, H), dtype=jnp.float32) * scale, 'alpha': jnp.float32(0.1)}
    _L0_xattn_all = _L0_xattn_setup()
    _L0_xattn_in = {k: v for k, v in _L0_xattn_all.items() if k in ('w_q', 'w_k', 'w_v', 'w_o', 'alpha')}
    del _L0_xattn_all

    def _L1_xattn_setup():
        import jax, jax.numpy as jnp
        import numpy as np
        B, C, CI, N = (16, 256, 128, 512)
        EPS = 1e-05

        def _conv1x1(w, b, x):
            return jnp.einsum('oc,bcn->bon', w, x) + b[None, :, None]
        key = jax.random.key(seed)
        ks = jax.random.split(key, 14)
        s = 0.02
        return {'x': jax.random.normal(ks[0], (B, C, N), jnp.float32), 'x_2': jax.random.normal(ks[1], (B, C, N), jnp.float32), 'theta_w': jax.random.normal(ks[2], (CI, C), jnp.float32) * s, 'theta_b': jax.random.normal(ks[3], (CI,), jnp.float32) * s, 'phi_w': jax.random.normal(ks[4], (CI, C), jnp.float32) * s, 'phi_b': jax.random.normal(ks[5], (CI,), jnp.float32) * s, 'g_w': jax.random.normal(ks[6], (CI, C), jnp.float32) * s, 'g_b': jax.random.normal(ks[7], (CI,), jnp.float32) * s, 'w_w': jax.random.normal(ks[8], (C, CI), jnp.float32) * s, 'w_b': jax.random.normal(ks[9], (C,), jnp.float32) * s, 'bn_gamma': jax.random.normal(ks[10], (C,), jnp.float32), 'bn_beta': jax.random.normal(ks[11], (C,), jnp.float32), 'bn_mean': jax.random.normal(ks[12], (C,), jnp.float32), 'bn_var': jax.random.uniform(ks[13], (C,), jnp.float32, 0.5, 1.5)}
    _L1_xattn_all = _L1_xattn_setup()
    _L1_xattn_in = {k: v for k, v in _L1_xattn_all.items() if k in ('theta_w', 'theta_b', 'phi_w', 'phi_b', 'g_w', 'g_b', 'w_w', 'w_b', 'bn_gamma', 'bn_beta', 'bn_mean', 'bn_var')}
    del _L1_xattn_all
    return {'x': x, 'ctx_2048': ctx_2048, 'L0_xattn_w_q': _L0_xattn_in['w_q'], 'L0_xattn_w_k': _L0_xattn_in['w_k'], 'L0_xattn_w_v': _L0_xattn_in['w_v'], 'L0_xattn_w_o': _L0_xattn_in['w_o'], 'L0_xattn_alpha': _L0_xattn_in['alpha'], 'L1_xattn_theta_w': _L1_xattn_in['theta_w'], 'L1_xattn_theta_b': _L1_xattn_in['theta_b'], 'L1_xattn_phi_w': _L1_xattn_in['phi_w'], 'L1_xattn_phi_b': _L1_xattn_in['phi_b'], 'L1_xattn_g_w': _L1_xattn_in['g_w'], 'L1_xattn_g_b': _L1_xattn_in['g_b'], 'L1_xattn_w_w': _L1_xattn_in['w_w'], 'L1_xattn_w_b': _L1_xattn_in['w_b'], 'L1_xattn_bn_gamma': _L1_xattn_in['bn_gamma'], 'L1_xattn_bn_beta': _L1_xattn_in['bn_beta'], 'L1_xattn_bn_mean': _L1_xattn_in['bn_mean'], 'L1_xattn_bn_var': _L1_xattn_in['bn_var']}

def reference(x, ctx_2048, L0_xattn_w_q, L0_xattn_w_k, L0_xattn_w_v, L0_xattn_w_o, L0_xattn_alpha, L1_xattn_theta_w, L1_xattn_theta_b, L1_xattn_phi_w, L1_xattn_phi_b, L1_xattn_g_w, L1_xattn_g_b, L1_xattn_w_w, L1_xattn_w_b, L1_xattn_bn_gamma, L1_xattn_bn_beta, L1_xattn_bn_mean, L1_xattn_bn_var):
    import jax
    import jax.numpy as jnp

    def _L0_xattn_ref(h_english, h_lojban, w_q, w_k, w_v, w_o, alpha):
        import jax, jax.numpy as jnp
        import numpy as np
        H = 512
        B, L, S = (4, 1024, 10)
        h = h_english.shape[-1]
        q = jnp.einsum('blh,oh->blo', h_english, w_q)
        k = jnp.einsum('bsh,oh->bso', h_lojban, w_k)
        v = jnp.einsum('bsh,oh->bso', h_lojban, w_v)
        scores = jnp.einsum('blh,bsh->bls', q, k) / jnp.sqrt(jnp.float32(h))
        probs = jax.nn.softmax(scores, axis=-1)
        context = jnp.einsum('bls,bsh->blh', probs, v)
        delta = jnp.einsum('blh,oh->blo', context, w_o)
        return h_english + alpha * delta

    def _L1_xattn_ref(x, x_2, theta_w, theta_b, phi_w, phi_b, g_w, g_b, w_w, w_b, bn_gamma, bn_beta, bn_mean, bn_var):
        import jax, jax.numpy as jnp
        import numpy as np
        B, C, CI, N = (16, 256, 128, 512)
        EPS = 1e-05

        def _conv1x1(w, b, x):
            return jnp.einsum('oc,bcn->bon', w, x) + b[None, :, None]
        g_x = _conv1x1(g_w, g_b, x_2).transpose(0, 2, 1)
        theta_x = _conv1x1(theta_w, theta_b, x).transpose(0, 2, 1)
        phi_x = _conv1x1(phi_w, phi_b, x_2)
        W = jnp.einsum('bnc,bcm->bnm', theta_x, phi_x) / phi_x.shape[-1]
        y = jnp.einsum('bnm,bmc->bnc', W, g_x).transpose(0, 2, 1)
        wy = _conv1x1(w_w, w_b, y)
        inv_std = jax.lax.rsqrt(bn_var + EPS)
        wy = bn_gamma[None, :, None] * (wy - bn_mean[None, :, None]) * inv_std[None, :, None] + bn_beta[None, :, None]
        return wy + x
    x = _L0_xattn_ref(x, ctx_2048, L0_xattn_w_q, L0_xattn_w_k, L0_xattn_w_v, L0_xattn_w_o, L0_xattn_alpha)
    x = _L1_xattn_ref(x, ctx_2048, L1_xattn_theta_w, L1_xattn_theta_b, L1_xattn_phi_w, L1_xattn_phi_b, L1_xattn_g_w, L1_xattn_g_b, L1_xattn_w_w, L1_xattn_w_b, L1_xattn_bn_gamma, L1_xattn_bn_beta, L1_xattn_bn_mean, L1_xattn_bn_var)
    return x

_drawn_inputs = setup_inputs


def setup_inputs(seed=0):
    import zlib

    import numpy as np

    out = dict(_drawn_inputs(seed))
    spreads = {}
    factors = {'L0_xattn_w_q': 5.035,
     'L0_xattn_w_k': 5.047,
     'L1_xattn_theta_w': 3.483,
     'L1_xattn_theta_b': 8.0,
     'L1_xattn_phi_w': 3.349,
     'L1_xattn_phi_b': 8.0,
     'L1_xattn_g_w': 3.542,
     'L1_xattn_g_b': 8.0,
     'L1_xattn_w_w': 3.276,
     'L1_xattn_w_b': 4.237}
    for name, (base, spread) in spreads.items():
        noise = np.random.default_rng([zlib.crc32(name.encode()), seed]).standard_normal(out[name].shape)
        drawn = base * np.exp(spread * noise) if base else spread * noise
        out[name] = jnp.asarray(drawn.astype(out[name].dtype))
    for name, factor in factors.items():
        out[name] = (out[name] * factor).astype(out[name].dtype)
    return out
```

```python
from contextlib import ExitStack

import numpy as np

import concourse.bass as bass
from concourse import mybir
from concourse.alu_op_type import AluOpType as ALU

ACT = mybir.ActivationFunctionType
AX = mybir.AxisListType
F32 = mybir.dt.float32
F32R = mybir.dt.float32r

P = 128
B, L, S, H = 16, 256, 256, 512
CI = 128
PAIRS = B // 2
KH, KL, KS = H // P, L // P, S // P
EPS = 1e-5
SCALE = float(H) ** -0.5
W_B, GAMMA, BETA, MEAN, VAR, THETA_B, N_COL = 0, 2, 4, 6, 8, 10, 11
ROW_GPHI_B, ROW_GAMMA, ROW_VAR, ROW_ALPHA, N_ROW = 0, 2 * CI, 2 * CI + L, 2 * CI + 2 * L, 2 * CI + 2 * L + 1


def two_stage_cross_attention(nc, x, x_t, ctx_n, ctx_t, w_q, w_k, w_v, w_o_t, gphi_w_t, theta_w_t,
                              w_w_t, cols, rows, out):
    with ExitStack() as stack:
        def sb(name, shape, dt=F32):
            return stack.enter_context(nc.sbuf_tensor(name, shape, dt))

        def split(name, shape):
            return sb(name + "_hi", shape, F32R), sb(name + "_lo", shape, F32R)

        def sem(name):
            return stack.enter_context(nc.semaphore(name))

        xT_raw = sb("xT_raw", [P, 2, KH, L])
        cT_raw = sb("cT_raw", [P, KH, 2, S])
        c_raw = sb("c_raw", [P, 2, KS, H])
        xb = sb("xb", [P, 2, KL, H])
        xT = split("xT", [P, 2, KH, L])
        cT = split("cT", [P, KH, 2, S])
        cn = split("cn", [P, 2, KS, H])
        tT = split("tT", [P, KH, 2, S])
        vo = split("vo", [P, 2, KS, H])
        x1 = split("x1", [P, 2, KL, H])
        probs = sb("probs", [P, 2, KL, S])
        pT = split("pT", [P, 2, KS, L])
        gphi = sb("gphi", [P, KH, 2 * CI])
        s_sb = sb("s_sb", [P, CI])
        t1 = split("t1", [P, L])
        theta = split("theta", [P, H])
        qk = split("qk", [P, KH, H])
        ov = split("ov", [P, KH, H])
        gphi_raw = sb("gphi_raw", [P, KS, 2 * CI])
        theta_raw = sb("theta_raw", [P, KL, CI])
        gphi_w = split("gphi_w", [P, KS, 2 * CI])
        theta_w = split("theta_w", [P, KL, CI])
        ww = sb("ww", [P, L])
        col = sb("col", [P, N_COL])
        row = sb("row", [P, N_ROW])
        std_row = sb("std_row", [P, L])
        bn_row = sb("bn_row", [P, L])
        std_col = sb("std_col", [P, KL])
        bn_col = sb("bn_col", [P, KL])
        out_bias = sb("out_bias", [P, KL])
        ident = sb("ident", [P, P])
        row_max = sb("row_max", [P, 2, KL])
        neg_max = sb("neg_max", [P, 2, KL])
        row_sum = sb("row_sum", [P, 2, KL])
        inv_sum = sb("inv_sum", [P, 2, KL])

        def by_k(t):
            return t.rearrange("p a k n -> p (a k) n")

        def as_k(t):
            return t.rearrange("p b k l -> p (b k l)").rearrange("p (k n) -> p k n", k=KH)

        wk_raw, wq_raw = by_k(xb[:]), as_k(cT_raw[:])
        wv_raw, wo_raw = as_k(xT_raw[:]), by_k(c_raw[:])
        wk = [as_k(t[:]) for t in tT]
        wq = [by_k(t[:]) for t in vo]
        wv = [by_k(t[:]) for t in x1]
        wo = [as_k(t[:]) for t in xT]

        bank = [stack.enter_context(nc.psum_tensor(f"bank{n}", [P, 512], F32)) for n in range(8)]
        SCORE_BANK = [0, 1]
        VO_BANK = [[2, 3], [5, 6]]
        PT_BANK = [4, 6]
        GPHI_BANK = [[7, 0], [3, 4]]
        DELTA_BANK = [[1, 2], [1, 2]]
        S_BANK = [5, 3]
        T1_BANK = [7, 6]
        THETA_BANK = [0, 1]
        OUT_BANK = [[4, 5], [4, 5]]
        TT_BANK = [7, 0, 2, 3]
        FIRST_T = [1, 2, 3, 0]

        w_loaded = [sem(f"w_loaded{n}") for n in range(2 * KH)]
        params_loaded = sem("params_loaded")
        small_w_loaded = sem("small_w_loaded")
        xT_loaded, cT_loaded, c_loaded = sem("xT_loaded"), sem("cT_loaded"), sem("c_loaded")
        x_loaded = [sem("x0_loaded"), sem("x1_loaded")]
        stored = [sem("out0_stored"), sem("out1_stored")]
        w_hi, w_lo = sem("w_hi"), sem("w_lo")
        small_hi, small_lo = sem("small_hi"), sem("small_lo")
        xT_hi, xT_lo = sem("xT_hi_made"), sem("xT_lo_made")
        cT_hi, cT_lo = sem("cT_hi_made"), sem("cT_lo_made")
        c_hi, c_lo = sem("c_hi_made"), sem("c_lo_made")
        var_made, std_made = sem("var_made"), sem("std_made")
        bn_step, ww_scaled = sem("bn_step"), sem("ww_scaled")
        ident_zeroed, ident_made = sem("ident_zeroed"), sem("ident_made")
        qk_done, qk_hi, qk_lo = sem("qk_done"), sem("qk_hi_made"), sem("qk_lo_made")
        ov_done, ov_hi, ov_lo = sem("ov_done"), sem("ov_hi_made"), sem("ov_lo_made")
        tT_done, tT_hi, tT_lo = sem("tT_done"), sem("tT_hi_made"), sem("tT_lo_made")
        scores_done = sem("scores_done")
        max_made, neg_max_made = sem("max_made"), sem("neg_max_made")
        probs_made, inv_sum_made = sem("probs_made"), sem("inv_sum_made")
        vo_done, vo_hi, vo_lo = sem("vo_done"), sem("vo_hi_made"), sem("vo_lo_made")
        pT_done, pT_hi, pT_lo = sem("pT_done"), sem("pT_hi_made"), sem("pT_lo_made")
        gphi_done, gphi_made = sem("gphi_done"), sem("gphi_made")
        delta_done, x1_made = sem("delta_done"), sem("x1_made")
        x1_hi, x1_lo = sem("x1_hi_made"), sem("x1_lo_made")
        s_done, s_made = sem("s_done"), sem("s_made")
        t1_done, t1_hi, t1_lo = sem("t1_done"), sem("t1_hi_made"), sem("t1_lo_made")
        theta_done, theta_hi, theta_lo = sem("theta_done"), sem("theta_hi_made"), sem("theta_lo_made")
        out_done, out_made = sem("out_done"), sem("out_made")

        def counts(eng, p, per_pair, offsets):
            return {n: per_pair * p + n if isinstance(p, int) else eng.snap(per_pair * p + n) for n in offsets}

        block = stack.enter_context(nc.Block())

        @block.sync
        def _(sp):
            def load_chunk(n, pairs):
                for dst, src, k in pairs:
                    sp.dma_start(dst[:, k, :], src[k * P:(k + 1) * P, :]).then_inc(w_loaded[n], 16)

            def load_xT(p):
                sp.dma_start(xT_raw[:], x_t[p]).then_inc(xT_loaded, 16)

            def load_cT(p):
                sp.dma_start(cT_raw[:], ctx_t[p]).then_inc(cT_loaded, 16)

            def load_c(p):
                sp.dma_start(c_raw[:], ctx_n[p]).then_inc(c_loaded, 16)

            def load_x(p, b):
                sp.dma_start(xb[:, b], x[p, :, b]).then_inc(x_loaded[b], 16)

            def store(p, b):
                sp.dma_start(out[p, :, b], xb[:, b]).then_inc(stored[b], 16)

            for k in range(KH):
                load_chunk(k, [(wk_raw, w_k, k), (wq_raw, w_q, k)])
            for k in range(KH):
                load_chunk(KH + k, [(wv_raw, w_v, k), (wo_raw, w_o_t, k)])
            sp.dma_start(col[:], cols).then_inc(params_loaded, 16)
            sp.dma_start(row[:], rows.partition_broadcast(P)).then_inc(params_loaded, 16)
            sp.dma_start(gphi_raw[:], gphi_w_t.rearrange("(k p) n -> p k n", p=P)).then_inc(small_w_loaded, 16)
            sp.dma_start(theta_raw[:], theta_w_t.rearrange("(k p) n -> p k n", p=P)).then_inc(small_w_loaded, 16)
            sp.dma_start(ww[:], w_w_t).then_inc(small_w_loaded, 16)
            sp.wait_ge(w_lo, 2 * KH)
            load_cT(0)
            load_x(0, 0)
            load_x(0, 1)
            sp.wait_ge(w_lo, 4 * KH)
            load_xT(0)
            load_c(0)
            sp.wait_ge(cT_lo, 2)
            load_cT(1)
            sp.wait_ge(xT_lo, 2)
            load_xT(1)
            sp.wait_ge(c_lo, 2)
            load_c(1)

            def pair(p, prefetch=True):
                two, four = counts(sp, p, 2, [4]), counts(sp, p, 4, [2, 4])
                if not (isinstance(p, int) and p == 0):
                    for b in range(2):
                        sp.wait_ge(stored[b], 16 * p)
                        load_x(p, b)
                if prefetch:
                    sp.wait_ge(xT_lo, two[4])
                    load_xT(p + 2)
                    sp.wait_ge(cT_lo, two[4])
                    load_cT(p + 2)
                    sp.wait_ge(c_lo, two[4])
                    load_c(p + 2)
                for b in range(2):
                    sp.wait_ge(out_made, four[2 * b + 2])
                    store(p, b)

            pair(0)
            with sp.Fori(1, PAIRS - 2) as p:
                pair(p)
            pair(PAIRS - 2, prefetch=False)
            pair(PAIRS - 1, prefetch=False)
            for b in range(2):
                sp.wait_ge(stored[b], 16 * PAIRS)

        @block.tensor
        def _(pe):
            def product(dst, lhsT, rhs, k_tiles):
                for k in range(k_tiles):
                    (ahi, alo), (bhi, blo) = lhsT(k), rhs(k)
                    pe.matmul(dst, ahi, bhi, start=(k == 0), stop=False)
                    pe.matmul(dst, ahi, blo, start=False, stop=False)
                    mm = pe.matmul(dst, alo, bhi, start=False, stop=(k == k_tiles - 1))
                return mm

            def cut(parts, *at):
                return tuple(t[at] for t in parts)

            every = slice(None)

            def tile(n):
                return slice(n * P, (n + 1) * P)

            for n, (lhs, rhs, done) in enumerate(((wk, wq, qk_done), (wv, wo, ov_done))):
                for k in range(KH):
                    pe.wait_ge(w_lo, 2 * (KH * n + k + 1))
                    for m in range(KH):
                        dst = bank[KH * n + m][:]
                        for a, b in ((0, 0), (0, 1), (1, 0)):
                            mm = pe.matmul(dst, lhs[a][:, k, tile(m)], rhs[b][:, k, :],
                                           start=(k == 0 and a == b), stop=(k == KH - 1 and a == 1))
                        if k == KH - 1:
                            mm.then_inc(done, 1)

            def t_tile(m):
                product(bank[TT_BANK[m]][:], lambda k: cut(qk, every, k, tile(m)),
                        lambda k: tuple(t[:, k].rearrange("p b s -> p (b s)") for t in cT),
                        KH).then_inc(tT_done, 1)

            def scores(b):
                for lt in range(KL):
                    mm = product(bank[SCORE_BANK[b]][:, lt * S:(lt + 1) * S],
                                 lambda k: cut(xT, every, b, k, tile(lt)),
                                 lambda k: cut(tT, every, k, b, every), KH)
                mm.then_inc(scores_done, 1)

            def values(b, st):
                product(bank[VO_BANK[b][st]][:], lambda k: cut(cT, every, k, b, tile(st)),
                        lambda k: cut(ov, every, k, every), KH).then_inc(vo_done, 1)

            def turn_probs(b):
                for st in range(KS):
                    for lt in range(KL):
                        at = st * L + lt * P
                        mm = pe.transpose(bank[PT_BANK[b]][:, at:at + P], probs[:, b, lt, tile(st)], ident[:])
                mm.then_inc(pT_done, 1)

            def g_and_phi(b, half):
                for j in range(2):
                    m = 2 * half + j
                    mm = product(bank[GPHI_BANK[b][half]][:, j * 2 * CI:(j + 1) * 2 * CI],
                                 lambda k: cut(cn, every, b, k, tile(m)),
                                 lambda k: cut(gphi_w, every, k, every), KS)
                mm.then_inc(gphi_done, 1)

            def delta(b, lt):
                product(bank[DELTA_BANK[b][lt]][:], lambda k: cut(pT, every, b, k, tile(lt)),
                        lambda k: cut(vo, every, b, k, every), KS).then_inc(delta_done, 1)

            def g_phi(b):
                for k in range(KH):
                    mm = pe.matmul(bank[S_BANK[b]][:, 0:CI], gphi[:, k, 0:CI], gphi[:, k, CI:2 * CI],
                                   start=(k == 0), stop=(k == KH - 1))
                mm.then_inc(s_done, 1)

            def w_g_phi(b):
                pe.matmul(bank[T1_BANK[b]][:, 0:L], s_sb[:], ww[:], start=True, stop=True).then_inc(t1_done, 1)

            def theta_rows(b):
                product(bank[THETA_BANK[b]][:], lambda k: cut(theta_w, every, k, every),
                        lambda k: cut(x1, every, b, k, every), KL).then_inc(theta_done, 1)

            def output(b, ct):
                product(bank[OUT_BANK[b][ct]][:], lambda k: cut(t1, every, tile(ct)),
                        lambda k: cut(theta, every, every), 1).then_inc(out_done, 1)

            pe.wait_ge(qk_lo, KH)
            pe.wait_ge(cT_lo, 2)
            for m in FIRST_T:
                if m == 0:
                    pe.wait_ge(ov_lo, KH)
                t_tile(m)

            def pair(p, first=False, last=False):
                two, four = counts(pe, p, 2, [0, 1, 2, 4]), counts(pe, p, 4, [0, 2, 4])
                pe.wait_ge(tT_lo, four[4])
                for b in range(2):
                    pe.wait_ge(xT_lo, two[b + 1])
                    if b == 1 and not first:
                        pe.wait_ge(theta_lo, two[0])
                    scores(b)
                for st in range(KS):
                    values(0, st)
                if first:
                    pe.wait_ge(ident_made, 1)
                else:
                    pe.wait_ge(out_made, four[0])
                pe.wait_ge(probs_made, two[1])
                turn_probs(0)
                for st in range(KS):
                    values(1, st)
                pe.wait_ge(c_lo, two[1])
                if first:
                    pe.wait_ge(small_lo, 2)
                for half in range(2):
                    g_and_phi(0, half)
                pe.wait_ge(probs_made, two[2])
                pe.wait_ge(vo_lo, four[2])
                pe.wait_ge(pT_lo, two[1])
                for lt in range(KL):
                    delta(0, lt)
                pe.wait_ge(c_lo, two[2])
                for half in range(2):
                    g_and_phi(1, half)
                pe.wait_ge(vo_lo, four[4])
                pe.wait_ge(gphi_made, four[2])
                g_phi(0)
                turn_probs(1)
                pe.wait_ge(s_made, two[1])
                if first:
                    pe.wait_ge(ww_scaled, 1)
                w_g_phi(0)
                pe.wait_ge(x1_lo, four[2])
                theta_rows(0)
                pe.wait_ge(pT_lo, two[2])
                for lt in range(KL):
                    delta(1, lt)
                pe.wait_ge(gphi_made, four[4])
                g_phi(1)
                pe.wait_ge(t1_lo, two[1])
                pe.wait_ge(theta_lo, two[1])
                for ct in range(KL):
                    output(0, ct)
                pe.wait_ge(s_made, two[2])
                w_g_phi(1)
                if not last:
                    pe.wait_ge(cT_lo, two[4])
                    t_tile(0)
                    t_tile(1)
                pe.wait_ge(x1_lo, four[4])
                theta_rows(1)
                if not last:
                    t_tile(2)
                    t_tile(3)
                pe.wait_ge(t1_lo, two[2])
                pe.wait_ge(theta_lo, two[2])
                pe.wait_ge(out_made, four[2])
                for ct in range(KL):
                    output(1, ct)

            pair(0, first=True)
            with pe.Fori(1, PAIRS - 1) as p:
                pair(p)
            pair(PAIRS - 1, last=True)

        @block.scalar
        def _(act):
            def hi(dst, src, made, **more):
                act.activation(dst, src, ACT.Identity, **more).then_inc(made, 1)

            for n in range(2 * KH):
                act.wait_ge(w_loaded[n], 32)
                for raw, parts in ((wk_raw, wk), (wq_raw, wq)) if n < KH else ((wv_raw, wv), (wo_raw, wo)):
                    hi(parts[0][:, n % KH, :], raw[:, n % KH, :], w_hi)

            def cT_parts(count):
                act.wait_ge(cT_loaded, count)
                for half in range(2):
                    hi(cT[0][:, 2 * half:2 * half + 2], cT_raw[:, 2 * half:2 * half + 2], cT_hi)

            def xT_part(b, count):
                act.wait_ge(xT_loaded, count)
                hi(xT[0][:, b], xT_raw[:, b], xT_hi)

            def c_part(b, count):
                act.wait_ge(c_loaded, count)
                hi(cn[0][:, b], c_raw[:, b], c_hi)

            def tT_part(m, count):
                act.wait_ge(tT_done, count)
                hi(tT[0][:, m], bank[TT_BANK[m]][:].rearrange("p (b s) -> p b s", b=2), tT_hi)

            cT_parts(16)
            for m in range(KH):
                act.wait_ge(qk_done, m + 1)
                hi(qk[0][:, m, :], bank[m][:], qk_hi)
            act.wait_ge(small_w_loaded, 48)
            hi(gphi_w[0][:], gphi_raw[:], small_hi)
            hi(theta_w[0][:], theta_raw[:], small_hi)
            act.wait_ge(var_made, 2)
            act.activation(std_row[:], bn_row[:], ACT.Sqrt).then_inc(std_made, 1)
            act.activation(std_col[:], bn_col[:], ACT.Sqrt).then_inc(std_made, 1)
            for b in range(2):
                c_part(b, 16)
            for m in range(KH):
                act.wait_ge(ov_done, m + 1)
                hi(ov[0][:, m, :], bank[KH + m][:], ov_hi, scale=row[:, ROW_ALPHA:ROW_ALPHA + 1])
            for b in range(2):
                xT_part(b, 16)
            for n, m in enumerate(FIRST_T):
                tT_part(m, n + 1)

            def pair(p, first=False, last=False):
                loads = counts(act, p, 16, [32])
                two, four = counts(act, p, 2, [-1, 0, 1, 2]), counts(act, p, 4, range(-2, 9))

                def exp(b):
                    act.wait_ge(neg_max_made, two[b + 1])
                    if not first:
                        act.wait_ge(pT_done, two[-1 + b])
                    for lt in range(KL):
                        e = act.activation(probs[:, b, lt], bank[SCORE_BANK[b]][:, lt * S:(lt + 1) * S], ACT.Exp,
                                           bias=neg_max[:, b, lt:lt + 1], scale=SCALE,
                                           accum_out=row_sum[:, b, lt:lt + 1])
                    e.then_inc(probs_made, 1)

                def vo_parts(b):
                    if not first:
                        act.wait_ge(delta_done, four[-2 + 2 * b])
                    for st in range(KS):
                        act.wait_ge(vo_done, four[2 * b + st + 1])
                        hi(vo[0][:, b, st], bank[VO_BANK[b][st]][:], vo_hi)

                def pT_part(b):
                    act.wait_ge(pT_done, two[b + 1])
                    hi(pT[0][:, b], bank[PT_BANK[b]][:].rearrange("p (t l) -> p t l", t=KS), pT_hi)

                def x1_parts(b):
                    if not first:
                        act.wait_ge(theta_done, two[-1 + b])
                    for lt in range(KL):
                        act.wait_ge(x1_made, four[2 * b + lt + 1])
                        hi(x1[0][:, b, lt], xb[:, b, lt], x1_hi)

                def t1_part(b):
                    act.wait_ge(t1_done, two[b + 1])
                    if b == 1 or not first:
                        act.wait_ge(out_done, four[2 * b])
                    hi(t1[0][:], bank[T1_BANK[b]][:, 0:L], t1_hi)

                def theta_part(b):
                    act.wait_ge(theta_done, two[b + 1])
                    hi(theta[0][:], bank[THETA_BANK[b]][:], theta_hi, bias=col[:, THETA_B:THETA_B + 1])

                exp(0)
                exp(1)
                if not last:
                    for b in range(2):
                        act.wait_ge(scores_done, two[b + 1])
                        xT_part(b, loads[32])
                vo_parts(0)
                pT_part(0)
                vo_parts(1)
                if not last:
                    act.wait_ge(vo_done, four[4])
                    cT_parts(loads[32])
                    act.wait_ge(gphi_done, four[2])
                    c_part(0, loads[32])
                x1_parts(0)
                pT_part(1)
                t1_part(0)
                if not last:
                    act.wait_ge(gphi_done, four[4])
                    c_part(1, loads[32])
                theta_part(0)
                x1_parts(1)
                t1_part(1)
                if not last:
                    tT_part(0, four[5])
                    tT_part(1, four[6])
                theta_part(1)
                if not last:
                    tT_part(2, four[7])
                    tT_part(3, four[8])

            pair(0, first=True)
            with act.Fori(1, PAIRS - 1) as p:
                pair(p)
            pair(PAIRS - 1, last=True)

        @block.vector
        def _(dve):
            def lo(parts, hi_made, count, at, src, made):
                dve.wait_ge(hi_made, count)
                dve.tensor_tensor(parts[1][at], src, parts[0][at].bitcast(F32), ALU.subtract).then_inc(made, 1)

            every = slice(None)
            for n in range(2 * KH):
                for j, (raw, parts) in enumerate(((wk_raw, wk), (wq_raw, wq)) if n < KH else ((wv_raw, wv), (wo_raw, wo))):
                    lo(parts, w_hi, 2 * n + j + 1, (every, n % KH), raw[:, n % KH, :], w_lo)

            def cT_parts(reached):
                for half in range(2):
                    at = (every, slice(2 * half, 2 * half + 2))
                    lo(cT, cT_hi, reached[half], at, cT_raw[at], cT_lo)

            def xT_part(b, count):
                lo(xT, xT_hi, count, (every, b), xT_raw[:, b], xT_lo)

            def c_part(b, count):
                lo(cn, c_hi, count, (every, b), c_raw[:, b], c_lo)

            def tT_part(m, count):
                lo(tT, tT_hi, count, (every, m), bank[TT_BANK[m]][:].rearrange("p (b s) -> p b s", b=2), tT_lo)

            cT_parts([1, 2])
            dve.wait_ge(params_loaded, 32)
            dve.tensor_scalar(bn_row[:], row[:, ROW_VAR:ROW_VAR + L], EPS, None, ALU.add).then_inc(var_made, 1)
            dve.tensor_scalar(bn_col[:], col[:, VAR:VAR + KL], EPS, None, ALU.add).then_inc(var_made, 1)
            for m in range(KH):
                lo(qk, qk_hi, m + 1, (every, m), bank[m][:], qk_lo)
            lo(gphi_w, small_hi, 1, (every,), gphi_raw[:], small_lo)
            lo(theta_w, small_hi, 2, (every,), theta_raw[:], small_lo)
            dve.wait_ge(std_made, 2)
            dve.reciprocal(bn_row[:], std_row[:]).then_inc(bn_step, 1)
            dve.reciprocal(bn_col[:], std_col[:]).then_inc(bn_step, 1)
            dve.wait_ge(bn_step, 2)
            dve.scalar_tensor_tensor(out=bn_row[:], in0=bn_row[:], scalar=1.0 / H, in1=row[:, ROW_GAMMA:ROW_GAMMA + L],
                                     op0=ALU.mult, op1=ALU.mult).then_inc(bn_step, 1)
            dve.tensor_tensor(bn_col[:], bn_col[:], col[:, GAMMA:GAMMA + KL], ALU.mult).then_inc(bn_step, 1)
            dve.tensor_tensor(out_bias[:], col[:, W_B:W_B + KL], col[:, MEAN:MEAN + KL], ALU.subtract).then_inc(bn_step, 1)
            dve.wait_ge(bn_step, 5)
            dve.tensor_tensor(ww[:], ww[:], bn_row[:], ALU.mult).then_inc(ww_scaled, 1)
            dve.tensor_tensor(out_bias[:], out_bias[:], bn_col[:], ALU.mult).then_inc(bn_step, 1)
            dve.wait_ge(bn_step, 6)
            dve.tensor_tensor(out_bias[:], out_bias[:], col[:, BETA:BETA + KL], ALU.add).then_inc(bn_step, 1)
            dve.wait_ge(bn_step, 7)
            for b in range(2):
                c_part(b, b + 1)
            for m in range(KH):
                dve.wait_ge(ov_hi, m + 1)
                dve.scalar_tensor_tensor(out=ov[1][:, m, :], in0=bank[KH + m][:], scalar=row[:, ROW_ALPHA:ROW_ALPHA + 1],
                                         in1=ov[0][:, m, :].bitcast(F32), op0=ALU.mult,
                                         op1=ALU.subtract).then_inc(ov_lo, 1)
            for b in range(2):
                xT_part(b, b + 1)
            for n, m in enumerate(FIRST_T):
                tT_part(m, n + 1)

            def pair(p, last=False):
                loads = counts(dve, p, 16, [16])
                two, four = counts(dve, p, 2, range(1, 5)), counts(dve, p, 4, range(1, 9))

                def row_maxima(b):
                    dve.wait_ge(scores_done, two[b + 1])
                    dve.tensor_reduce(row_max[:, b], bank[SCORE_BANK[b]][:].rearrange("p (t s) -> p t s", t=KL),
                                      AX.X, ALU.max).then_inc(max_made, 1)
                    dve.wait_ge(max_made, two[b + 1])
                    dve.tensor_scalar(neg_max[:, b], row_max[:, b], -SCALE, None, ALU.mult).then_inc(neg_max_made, 1)

                def invert_sums(b):
                    dve.wait_ge(probs_made, two[b + 1])
                    dve.reciprocal(inv_sum[:, b], row_sum[:, b]).then_inc(inv_sum_made, 1)

                def vo_parts(b):
                    for st in range(KS):
                        lo(vo, vo_hi, four[2 * b + st + 1], (every, b, st), bank[VO_BANK[b][st]][:], vo_lo)

                def pT_part(b):
                    lo(pT, pT_hi, two[b + 1], (every, b),
                       bank[PT_BANK[b]][:].rearrange("p (t l) -> p t l", t=KS), pT_lo)

                def gphi_rows(b):
                    for half in range(2):
                        dve.wait_ge(gphi_done, four[2 * b + half + 1])
                        for j in range(2):
                            g = dve.tensor_tensor(gphi[:, 2 * half + j], bank[GPHI_BANK[b][half]][:, j * 2 * CI:(j + 1) * 2 * CI],
                                                  row[:, ROW_GPHI_B:ROW_GPHI_B + 2 * CI], ALU.add)
                        g.then_inc(gphi_made, 1)

                def x1_rows(b):
                    dve.wait_ge(x_loaded[b], loads[16])
                    dve.wait_ge(inv_sum_made, two[b + 1])
                    for lt in range(KL):
                        dve.wait_ge(delta_done, four[2 * b + lt + 1])
                        dve.scalar_tensor_tensor(out=xb[:, b, lt], in0=bank[DELTA_BANK[b][lt]][:],
                                                 scalar=inv_sum[:, b, lt:lt + 1], in1=xb[:, b, lt],
                                                 op0=ALU.mult, op1=ALU.add).then_inc(x1_made, 1)
                    for lt in range(KL):
                        lo(x1, x1_hi, four[2 * b + lt + 1], (every, b, lt), xb[:, b, lt], x1_lo)

                def s_rows(b):
                    dve.wait_ge(s_done, two[b + 1])
                    dve.tensor_copy(s_sb[:], bank[S_BANK[b]][:, 0:CI]).then_inc(s_made, 1)

                def t1_part(b):
                    lo(t1, t1_hi, two[b + 1], (every,), bank[T1_BANK[b]][:, 0:L], t1_lo)

                def theta_part(b):
                    dve.wait_ge(theta_hi, two[b + 1])
                    dve.scalar_tensor_tensor(out=theta[1][:], in0=bank[THETA_BANK[b]][:],
                                             scalar=col[:, THETA_B:THETA_B + 1], in1=theta[0][:].bitcast(F32),
                                             op0=ALU.add, op1=ALU.subtract).then_inc(theta_lo, 1)

                def out_rows(b):
                    for ct in range(KL):
                        dve.wait_ge(out_done, four[2 * b + ct + 1])
                        dve.scalar_tensor_tensor(out=xb[:, b, ct], in0=bank[OUT_BANK[b][ct]][:],
                                                 scalar=out_bias[:, ct:ct + 1], in1=xb[:, b, ct],
                                                 op0=ALU.add, op1=ALU.add).then_inc(out_made, 1)

                row_maxima(0)
                row_maxima(1)
                if not last:
                    for b in range(2):
                        xT_part(b, two[b + 3])
                invert_sums(0)
                vo_parts(0)
                invert_sums(1)
                pT_part(0)
                vo_parts(1)
                if not last:
                    cT_parts([two[3], two[4]])
                gphi_rows(0)
                x1_rows(0)
                if not last:
                    c_part(0, two[3])
                s_rows(0)
                pT_part(1)
                t1_part(0)
                gphi_rows(1)
                theta_part(0)
                if not last:
                    c_part(1, two[4])
                x1_rows(1)
                s_rows(1)
                out_rows(0)
                t1_part(1)
                if not last:
                    tT_part(0, four[5])
                    tT_part(1, four[6])
                theta_part(1)
                if not last:
                    tT_part(2, four[7])
                    tT_part(3, four[8])
                out_rows(1)

            pair(0)
            with dve.Fori(1, PAIRS - 1) as p:
                pair(p)
            pair(PAIRS - 1, last=True)

        @block.gpsimd
        def _(pool):
            pool.memset(ident[:], 0.0).then_inc(ident_zeroed, 1)
            pool.wait_ge(ident_zeroed, 1)
            pool.affine_select(out=ident[:], in_=ident[:], compare_op=ALU.not_equal, fill=1.0, base=0,
                               pattern=[[-1, P]], channel_multiplier=1).then_inc(ident_made, 1)


def kernel(**inputs):
    import concourse.bacc as bacc
    from concourse.bass_utils import run_bass_kernel_spmd

    a = {n: np.asarray(v) for n, v in inputs.items()}

    def pairs(t, rows_of):
        t = t.reshape(PAIRS, 2, rows_of, P, t.shape[-1])
        return t.transpose(0, 3, 1, 2, 4)

    x, ctx = a["x"], a["ctx_2048"]
    l1 = "L1_xattn_"
    per_channel = [a[l1 + n].reshape(KL, P).T for n in ("w_b", "bn_gamma", "bn_beta", "bn_mean", "bn_var")]
    arrays = {
        "x": pairs(x, KL),
        "x_t": pairs(x.transpose(0, 2, 1), KH),
        "ctx_n": pairs(ctx, KS),
        "ctx_t": pairs(ctx.transpose(0, 2, 1), KH).transpose(0, 1, 3, 2, 4),
        "w_q": a["L0_xattn_w_q"],
        "w_k": a["L0_xattn_w_k"],
        "w_v": a["L0_xattn_w_v"],
        "w_o_t": a["L0_xattn_w_o"].T,
        "gphi_w_t": np.concatenate([a[l1 + "g_w"], a[l1 + "phi_w"]]).T,
        "theta_w_t": a[l1 + "theta_w"].T,
        "w_w_t": a[l1 + "w_w"].T,
        "cols": np.concatenate(per_channel + [a[l1 + "theta_b"].reshape(CI, 1)], axis=1),
        "rows": np.concatenate([a[l1 + "g_b"], a[l1 + "phi_b"], a[l1 + "bn_gamma"], a[l1 + "bn_var"],
                                a["L0_xattn_alpha"].reshape(1)]),
    }
    arrays = {n: np.ascontiguousarray(v) for n, v in arrays.items()}
    nc = bacc.Bacc("TRN2", target_bir_lowering=False, num_devices=1)
    args = {n: nc.dram_tensor(n, v.shape, F32, kind="ExternalInput").ap() for n, v in arrays.items()}
    out = nc.dram_tensor("out", (PAIRS, P, 2, KL, H), F32, kind="ExternalOutput").ap()
    two_stage_cross_attention(nc, out=out, **args)
    got = run_bass_kernel_spmd(nc, [arrays], core_ids=[0]).results[0]["out"]
    return got.transpose(0, 2, 3, 1, 4).reshape(B, L, H)
```

```python
from contextlib import ExitStack

import numpy as np

import concourse.bass as bass
from concourse import mybir
from concourse.alu_op_type import AluOpType as ALU

ACT = mybir.ActivationFunctionType
AX = mybir.AxisListType
F32 = mybir.dt.float32
F32R = mybir.dt.float32r

P = 128
B, L, S, H = 16, 256, 256, 512
CI = 128
PAIRS = B // 2
KH, KL, KS = H // P, L // P, S // P
EPS = 1e-5
IDLE_PRODUCTS = 9
SCALE = float(H) ** -0.5
W_B, GAMMA, BETA, MEAN, VAR, THETA_B, N_COL = 0, 2, 4, 6, 8, 10, 11
ROW_GPHI_B, ROW_GAMMA, ROW_VAR, ROW_ALPHA, N_ROW = 0, 2 * CI, 2 * CI + L, 2 * CI + 2 * L, 2 * CI + 2 * L + 1


def two_stage_cross_attention(nc, x, x_t, ctx_n, ctx_t, w_q, w_k, w_v, w_o_t, gphi_w_t, theta_w_t,
                              w_w_t, cols, rows, out):
    with ExitStack() as stack:
        def sb(name, shape, dt=F32):
            return stack.enter_context(nc.sbuf_tensor(name, shape, dt))

        def split(name, shape):
            return sb(name + "_hi", shape, F32R), sb(name + "_lo", shape, F32R)

        def sem(name):
            return stack.enter_context(nc.semaphore(name))

        xT_raw = sb("xT_raw", [P, 2, KH, L])
        cT_raw = sb("cT_raw", [P, KH, 2, S])
        c_raw = sb("c_raw", [P, 2, KS, H])
        xb = sb("xb", [P, 2, KL, H])
        xT = split("xT", [P, 2, KH, L])
        cT = split("cT", [P, KH, 2, S])
        cn = split("cn", [P, 2, KS, H])
        tT = split("tT", [P, KH, 2, S])
        vo = split("vo", [P, 2, KS, H])
        x1 = split("x1", [P, 2, KL, H])
        probs = sb("probs", [P, 2, KL, S])
        pT = split("pT", [P, 2, KS, L])
        gphi = sb("gphi", [P, KH, 2 * CI])
        s = split("s", [P, CI])
        t1 = split("t1", [P, 2, L])
        theta = split("theta", [P, 2, H])
        qk = split("qk", [P, KH, H])
        ov = split("ov", [P, KH, H])
        gphi_raw = sb("gphi_raw", [P, KS, 2 * CI])
        theta_raw = sb("theta_raw", [P, KL, CI])
        gphi_w = split("gphi_w", [P, KS, 2 * CI])
        theta_w = split("theta_w", [P, KL, CI])
        ww_raw = sb("ww_raw", [P, L])
        ww = split("ww", [P, L])
        idle = sb("idle", [P, 512], mybir.dt.bfloat16)
        col = sb("col", [P, N_COL])
        row = sb("row", [P, N_ROW])
        std_row = sb("std_row", [P, L])
        bn_row = sb("bn_row", [P, L])
        std_col = sb("std_col", [P, KL])
        bn_col = sb("bn_col", [P, KL])
        out_bias = sb("out_bias", [P, KL])
        ident = sb("ident", [P, P])
        row_max = sb("row_max", [P, 2, KL])
        neg_max = sb("neg_max", [P, 2, KL])
        row_sum = sb("row_sum", [P, 2, KL])
        inv_sum = sb("inv_sum", [P, 2, KL])

        def by_k(t):
            return t.rearrange("p a k n -> p (a k) n")

        def as_k(t):
            return t.rearrange("p b k l -> p (b k l)").rearrange("p (k n) -> p k n", k=KH)

        wk_raw, wq_raw = by_k(xb[:]), as_k(cT_raw[:])
        wv_raw, wo_raw = as_k(xT_raw[:]), by_k(c_raw[:])
        wk = [as_k(t[:]) for t in tT]
        wq = [by_k(t[:]) for t in vo]
        wv = [by_k(t[:]) for t in x1]
        wo = [as_k(t[:]) for t in xT]

        bank = [stack.enter_context(nc.psum_tensor(f"bank{n}", [P, 512], F32)) for n in range(8)]
        SCORE_BANK = [0, 1]
        VO_BANK = [[2, 3], [5, 6]]
        PT_BANK = [4, 6]
        GPHI_BANK = [[7, 0], [3, 4]]
        DELTA_BANK = [[1, 2], [1, 2]]
        S_BANK = [5, 3]
        T1_BANK = [7, 6]
        THETA_BANK = [0, 1]
        OUT_BANK = [[4, 5], [4, 5]]
        LAST_OUT_BANK = [[4, 5], [7, 0]]
        TT_BANK = [7, 0, 2, 3]
        FIRST_T = [1, 2, 3, 0]

        w_loaded = [sem(f"w_loaded{n}") for n in range(2 * KH)]
        params_loaded = sem("params_loaded")
        small_w_loaded = sem("small_w_loaded")
        xT_loaded, cT_loaded, c_loaded = sem("xT_loaded"), sem("cT_loaded"), sem("c_loaded")
        x_loaded = [sem("x0_loaded"), sem("x1_loaded")]
        stored = [sem("out0_stored"), sem("out1_stored")]
        tile_stored = sem("out_tile_stored")
        lhs_hi, rhs_hi = sem("w_lhs_hi"), sem("w_rhs_hi")
        w_lo = sem("w_lo")
        small_hi, small_lo = sem("small_hi"), sem("small_lo")
        xT_hi, xT_lo = sem("xT_hi_made"), sem("xT_lo_made")
        cT_hi, cT_lo = sem("cT_hi_made"), sem("cT_lo_made")
        c_hi, c_lo = sem("c_hi_made"), sem("c_lo_made")
        var_made, std_made = sem("var_made"), sem("std_made")
        bn_step, ww_scaled = sem("bn_step"), sem("ww_scaled")
        ww_hi, ww_lo = sem("ww_hi_made"), sem("ww_lo_made")
        idle_zeroed = sem("idle_zeroed")
        ident_zeroed, ident_made = sem("ident_zeroed"), sem("ident_made")
        qk_done, qk_hi, qk_lo = sem("qk_done"), sem("qk_hi_made"), sem("qk_lo_made")
        ov_done, ov_hi, ov_lo = sem("ov_done"), sem("ov_hi_made"), sem("ov_lo_made")
        tT_done, tT_hi, tT_lo = sem("tT_done"), sem("tT_hi_made"), sem("tT_lo_made")
        scores_done = sem("scores_done")
        max_made, neg_max_made = sem("max_made"), sem("neg_max_made")
        probs_made, inv_sum_made = sem("probs_made"), sem("inv_sum_made")
        vo_done, vo_hi, vo_lo = sem("vo_done"), sem("vo_hi_made"), sem("vo_lo_made")
        pT_done, pT_hi, pT_lo = sem("pT_done"), sem("pT_hi_made"), sem("pT_lo_made")
        gphi_done, gphi_made = sem("gphi_done"), sem("gphi_made")
        delta_done, x1_made = sem("delta_done"), sem("x1_made")
        x1_hi, x1_lo = sem("x1_hi_made"), sem("x1_lo_made")
        s_done, s_hi, s_lo = sem("s_done"), sem("s_hi_made"), sem("s_lo_made")
        t1_done, t1_hi, t1_lo = sem("t1_done"), sem("t1_hi_made"), sem("t1_lo_made")
        theta_done, theta_hi, theta_lo = sem("theta_done"), sem("theta_hi_made"), sem("theta_lo_made")
        out_done, out_made = sem("out_done"), sem("out_made")

        def counts(eng, p, per_pair, offsets):
            return {n: per_pair * p + n if isinstance(p, int) else eng.snap(per_pair * p + n) for n in offsets}

        block = stack.enter_context(nc.Block())

        @block.sync
        def _(sp):
            def load_chunk(n, pairs):
                for dst, src, k in pairs:
                    sp.dma_start(dst[:, k, :], src[k * P:(k + 1) * P, :]).then_inc(w_loaded[n], 16)

            def load_xT(p):
                sp.dma_start(xT_raw[:], x_t[p]).then_inc(xT_loaded, 16)

            def load_cT(p):
                sp.dma_start(cT_raw[:], ctx_t[p]).then_inc(cT_loaded, 16)

            def load_c(p):
                sp.dma_start(c_raw[:], ctx_n[p]).then_inc(c_loaded, 16)

            def load_x(p, b):
                sp.dma_start(xb[:, b], x[p, :, b]).then_inc(x_loaded[b], 16)

            def store(p, b):
                sp.dma_start(out[p, :, b], xb[:, b]).then_inc(stored[b], 16)

            def store_tile(p, b, ct):
                sp.dma_start(out[p, :, b, ct], xb[:, b, ct]).then_inc(tile_stored, 16)

            for k in range(KH):
                load_chunk(k, [(wk_raw, w_k, k), (wq_raw, w_q, k)])
            sp.dma_start(col[:], cols).then_inc(params_loaded, 16)
            sp.dma_start(row[:], rows.partition_broadcast(P)).then_inc(params_loaded, 16)
            for k in range(KH):
                load_chunk(KH + k, [(wv_raw, w_v, k), (wo_raw, w_o_t, k)])
            sp.dma_start(gphi_raw[:], gphi_w_t.rearrange("(k p) n -> p k n", p=P)).then_inc(small_w_loaded, 16)
            sp.dma_start(theta_raw[:], theta_w_t.rearrange("(k p) n -> p k n", p=P)).then_inc(small_w_loaded, 16)
            sp.dma_start(ww_raw[:], w_w_t).then_inc(small_w_loaded, 16)
            sp.wait_ge(w_lo, 2 * KH)
            load_cT(0)
            sp.wait_ge(w_lo, 4 * KH)
            load_c(0)
            load_xT(0)
            load_x(0, 0)
            load_x(0, 1)
            sp.wait_ge(cT_lo, 2)
            load_cT(1)
            sp.wait_ge(xT_lo, 2)
            load_xT(1)
            sp.wait_ge(c_lo, 2)
            load_c(1)

            def pair(p, prefetch=True, last=False):
                two, four = counts(sp, p, 2, [4]), counts(sp, p, 4, [2, 3, 4])
                if not (isinstance(p, int) and p == 0):
                    for b in range(2):
                        sp.wait_ge(stored[b], 16 * p)
                        load_x(p, b)
                if prefetch:
                    sp.wait_ge(xT_lo, two[4])
                    load_xT(p + 2)
                    sp.wait_ge(cT_lo, two[4])
                    load_cT(p + 2)
                    sp.wait_ge(c_lo, two[4])
                    load_c(p + 2)
                sp.wait_ge(out_made, four[2])
                store(p, 0)
                if last:
                    for ct in range(KL):
                        sp.wait_ge(out_made, four[3 + ct])
                        store_tile(p, 1, ct)
                else:
                    sp.wait_ge(out_made, four[4])
                    store(p, 1)

            pair(0)
            with sp.Fori(1, PAIRS - 2) as p:
                pair(p)
            pair(PAIRS - 2, prefetch=False)
            pair(PAIRS - 1, prefetch=False, last=True)
            sp.wait_ge(stored[0], 16 * PAIRS)
            sp.wait_ge(stored[1], 16 * (PAIRS - 1))
            sp.wait_ge(tile_stored, 16 * KL)

        @block.tensor
        def _(pe):
            def product(dst, lhsT, rhs, k_tiles):
                for k in range(k_tiles):
                    (ahi, alo), (bhi, blo) = lhsT(k), rhs(k)
                    pe.matmul(dst, ahi, bhi, start=(k == 0), stop=False)
                    pe.matmul(dst, ahi, blo, start=False, stop=False)
                    mm = pe.matmul(dst, alo, bhi, start=False, stop=(k == k_tiles - 1))
                return mm

            def cut(parts, *at):
                return tuple(t[at] for t in parts)

            every = slice(None)

            def tile(n):
                return slice(n * P, (n + 1) * P)

            pe.wait_ge(idle_zeroed, 1)
            for _ in range(IDLE_PRODUCTS):
                pe.matmul(bank[7][:], idle[:, 0:P], idle[:], start=True, stop=True)

            for n, (lhs, rhs, done) in enumerate(((wk, wq, qk_done), (wv, wo, ov_done))):
                for k in range(KH):
                    for a, b in ((0, 0), (0, 1), (1, 0)):
                        if a == b:
                            pe.wait_ge(lhs_hi, KH * n + k + 1)
                            pe.wait_ge(rhs_hi, KH * n + k + 1)
                        elif b == 1:
                            pe.wait_ge(w_lo, 2 * (KH * n + k + 1))
                        for m in range(KH):
                            mm = pe.matmul(bank[KH * n + m][:], lhs[a][:, k, tile(m)], rhs[b][:, k, :],
                                           start=(k == 0 and a == b), stop=(k == KH - 1 and a == 1))
                            if k == KH - 1 and a == 1:
                                mm.then_inc(done, 1)

            def t_tile(m):
                product(bank[TT_BANK[m]][:], lambda k: cut(qk, every, k, tile(m)),
                        lambda k: tuple(t[:, k].rearrange("p b s -> p (b s)") for t in cT),
                        KH).then_inc(tT_done, 1)

            def scores(b, order, last_t=None):
                for lt in range(KL):
                    dst = bank[SCORE_BANK[b]][:, lt * S:(lt + 1) * S]
                    for n, k in enumerate(order):
                        if last_t is not None and lt == 0 and n == KH - 1:
                            pe.wait_ge(tT_lo, last_t)
                        x_hi, x_lo = cut(xT, every, b, k, tile(lt))
                        t_hi, t_lo = cut(tT, every, k, b, every)
                        pe.matmul(dst, x_hi, t_hi, start=(n == 0), stop=False)
                        pe.matmul(dst, x_hi, t_lo, start=False, stop=False)
                        mm = pe.matmul(dst, x_lo, t_hi, start=False, stop=(n == KH - 1))
                mm.then_inc(scores_done, 1)

            def values(b, st):
                product(bank[VO_BANK[b][st]][:], lambda k: cut(cT, every, k, b, tile(st)),
                        lambda k: cut(ov, every, k, every), KH).then_inc(vo_done, 1)

            def turn_probs(b):
                for st in range(KS):
                    for lt in range(KL):
                        at = st * L + lt * P
                        mm = pe.transpose(bank[PT_BANK[b]][:, at:at + P], probs[:, b, lt, tile(st)], ident[:])
                mm.then_inc(pT_done, 1)

            def g_and_phi(b, half):
                for j in range(2):
                    m = 2 * half + j
                    mm = product(bank[GPHI_BANK[b][half]][:, j * 2 * CI:(j + 1) * 2 * CI],
                                 lambda k: cut(cn, every, b, k, tile(m)),
                                 lambda k: cut(gphi_w, every, k, every), KS)
                mm.then_inc(gphi_done, 1)

            def delta(b, lt):
                product(bank[DELTA_BANK[b][lt]][:], lambda k: cut(pT, every, b, k, tile(lt)),
                        lambda k: cut(vo, every, b, k, every), KS).then_inc(delta_done, 1)

            def g_phi(b):
                for k in range(KH):
                    mm = pe.matmul(bank[S_BANK[b]][:, 0:CI], gphi[:, k, 0:CI], gphi[:, k, CI:2 * CI],
                                   start=(k == 0), stop=(k == KH - 1))
                mm.then_inc(s_done, 1)

            def w_g_phi(b):
                product(bank[T1_BANK[b]][:, 0:L], lambda k: cut(s, every, every),
                        lambda k: cut(ww, every, every), 1).then_inc(t1_done, 1)

            def theta_rows(b):
                product(bank[THETA_BANK[b]][:], lambda k: cut(theta_w, every, k, every),
                        lambda k: cut(x1, every, b, k, every), KL).then_inc(theta_done, 1)

            def output(b, ct, banks=OUT_BANK):
                product(bank[banks[b][ct]][:], lambda k: cut(t1, every, b, tile(ct)),
                        lambda k: cut(theta, every, b, every), 1).then_inc(out_done, 1)

            pe.wait_ge(qk_lo, KH)
            pe.wait_ge(cT_lo, 2)
            for m in FIRST_T:
                if m == 0:
                    pe.wait_ge(ov_lo, KH)
                t_tile(m)

            def pair(p, first=False, last=False):
                two, four = counts(pe, p, 2, [0, 1, 2, 4]), counts(pe, p, 4, [0, 2, 3, 4])
                pe.wait_ge(tT_lo, four[3])
                pe.wait_ge(xT_lo, two[1])
                scores(0, FIRST_T if first else range(KH), four[4])
                pe.wait_ge(xT_lo, two[2])
                if not first:
                    pe.wait_ge(theta_lo, two[0])
                scores(1, range(KH))
                for st in range(KS):
                    values(0, st)
                if first:
                    pe.wait_ge(ident_made, 1)
                else:
                    pe.wait_ge(out_made, four[0])
                pe.wait_ge(probs_made, two[1])
                turn_probs(0)
                for st in range(KS):
                    values(1, st)
                pe.wait_ge(c_lo, two[1])
                if first:
                    pe.wait_ge(small_lo, 2)
                for half in range(2):
                    g_and_phi(0, half)
                pe.wait_ge(probs_made, two[2])
                pe.wait_ge(vo_lo, four[2])
                pe.wait_ge(pT_lo, two[1])
                for lt in range(KL):
                    delta(0, lt)
                pe.wait_ge(c_lo, two[2])
                for half in range(2):
                    g_and_phi(1, half)
                pe.wait_ge(vo_lo, four[4])
                pe.wait_ge(gphi_made, four[2])
                g_phi(0)
                turn_probs(1)
                pe.wait_ge(x1_lo, four[2])
                theta_rows(0)
                pe.wait_ge(s_lo, two[1])
                if first:
                    pe.wait_ge(ww_lo, 1)
                w_g_phi(0)
                pe.wait_ge(pT_lo, two[2])
                for lt in range(KL):
                    delta(1, lt)
                pe.wait_ge(gphi_made, four[4])
                g_phi(1)

                if not last:
                    pe.wait_ge(t1_lo, two[1])
                    pe.wait_ge(theta_lo, two[1])
                    for ct in range(KL):
                        output(0, ct)
                    pe.wait_ge(s_lo, two[2])
                    w_g_phi(1)
                    pe.wait_ge(cT_lo, two[4])
                    t_tile(0)
                    t_tile(1)
                    pe.wait_ge(x1_lo, four[4])
                    theta_rows(1)
                    t_tile(2)
                    t_tile(3)
                    pe.wait_ge(t1_lo, two[2])
                    pe.wait_ge(theta_lo, two[2])
                    pe.wait_ge(out_made, four[2])
                    for ct in range(KL):
                        output(1, ct)
                else:
                    pe.wait_ge(t1_lo, two[1])
                    pe.wait_ge(theta_lo, two[1])
                    for ct in range(KL):
                        output(0, ct)
                    pe.wait_ge(s_lo, two[2])
                    w_g_phi(1)
                    pe.wait_ge(x1_lo, four[4])
                    theta_rows(1)
                    pe.wait_ge(t1_lo, two[2])
                    pe.wait_ge(theta_lo, two[2])
                    for ct in range(KL):
                        output(1, ct, LAST_OUT_BANK)

            pair(0, first=True)
            with pe.Fori(1, PAIRS - 1) as p:
                pair(p)
            pair(PAIRS - 1, last=True)

        @block.scalar
        def _(act):
            def hi(dst, src, made, **more):
                act.activation(dst, src, ACT.Identity, **more).then_inc(made, 1)

            for n in range(2 * KH):
                act.wait_ge(w_loaded[n], 32)
                raw, parts = (wk_raw, wk) if n < KH else (wv_raw, wv)
                hi(parts[0][:, n % KH, :], raw[:, n % KH, :], lhs_hi)

            def cT_parts(count):
                act.wait_ge(cT_loaded, count)
                for half in range(2):
                    hi(cT[0][:, 2 * half:2 * half + 2], cT_raw[:, 2 * half:2 * half + 2], cT_hi)

            def xT_part(b, count):
                act.wait_ge(xT_loaded, count)
                hi(xT[0][:, b], xT_raw[:, b], xT_hi)

            def c_part(b, count):
                act.wait_ge(c_loaded, count)
                hi(cn[0][:, b], c_raw[:, b], c_hi)

            def tT_part(m, count):
                act.wait_ge(tT_done, count)
                hi(tT[0][:, m], bank[TT_BANK[m]][:].rearrange("p (b s) -> p b s", b=2), tT_hi)

            for m in range(KH):
                act.wait_ge(qk_done, m + 1)
                hi(qk[0][:, m, :], bank[m][:], qk_hi)
            cT_parts(16)
            act.wait_ge(small_w_loaded, 48)
            hi(gphi_w[0][:], gphi_raw[:], small_hi)
            hi(theta_w[0][:], theta_raw[:], small_hi)
            act.wait_ge(var_made, 2)
            act.activation(std_row[:], bn_row[:], ACT.Sqrt).then_inc(std_made, 1)
            act.activation(std_col[:], bn_col[:], ACT.Sqrt).then_inc(std_made, 1)
            act.wait_ge(ov_done, KH)
            for m in range(KH):
                hi(ov[0][:, m, :], bank[KH + m][:], ov_hi, scale=row[:, ROW_ALPHA:ROW_ALPHA + 1])
            for b in range(2):
                xT_part(b, 16)
            act.wait_ge(ww_scaled, 1)
            hi(ww[0][:], ww_raw[:], ww_hi)
            for n, m in enumerate(FIRST_T[:-1]):
                tT_part(m, n + 1)
            for b in range(2):
                c_part(b, 16)
            tT_part(FIRST_T[-1], KH)

            def pair(p, first=False, last=False):
                loads = counts(act, p, 16, [32])
                two, four = counts(act, p, 2, [-1, 0, 1, 2]), counts(act, p, 4, range(-2, 9))

                def exp(b):
                    act.wait_ge(neg_max_made, two[b + 1])
                    if not first:
                        act.wait_ge(pT_done, two[-1 + b])
                    for lt in range(KL):
                        e = act.activation(probs[:, b, lt], bank[SCORE_BANK[b]][:, lt * S:(lt + 1) * S], ACT.Exp,
                                           bias=neg_max[:, b, lt:lt + 1], scale=SCALE,
                                           accum_out=row_sum[:, b, lt:lt + 1])
                    e.then_inc(probs_made, 1)

                def vo_parts(b):
                    if not first:
                        act.wait_ge(delta_done, four[-2 + 2 * b])
                    for st in range(KS):
                        act.wait_ge(vo_done, four[2 * b + st + 1])
                        hi(vo[0][:, b, st], bank[VO_BANK[b][st]][:], vo_hi)

                def pT_part(b):
                    act.wait_ge(pT_done, two[b + 1])
                    hi(pT[0][:, b], bank[PT_BANK[b]][:].rearrange("p (t l) -> p t l", t=KS), pT_hi)

                def x1_part(b, lt):
                    if lt == 0 and not first:
                        act.wait_ge(theta_done, two[-1 + b])
                    act.wait_ge(x1_made, four[2 * b + lt + 1])
                    hi(x1[0][:, b, lt], xb[:, b, lt], x1_hi)

                def s_part(b):
                    act.wait_ge(s_done, two[b + 1])
                    hi(s[0][:], bank[S_BANK[b]][:, 0:CI], s_hi)

                def t1_part(b):
                    act.wait_ge(t1_done, two[b + 1])
                    hi(t1[0][:, b], bank[T1_BANK[b]][:, 0:L], t1_hi)

                def theta_part(b):
                    act.wait_ge(theta_done, two[b + 1])
                    if not first:
                        act.wait_ge(out_done, four[2 * b - 2])
                    hi(theta[0][:, b], bank[THETA_BANK[b]][:], theta_hi, bias=col[:, THETA_B:THETA_B + 1])

                exp(0)
                exp(1)
                if not last:
                    for b in range(2):
                        act.wait_ge(scores_done, two[b + 1])
                        xT_part(b, loads[32])
                vo_parts(0)
                pT_part(0)
                vo_parts(1)
                if not last:
                    act.wait_ge(vo_done, four[4])
                    cT_parts(loads[32])
                x1_part(0, 0)
                x1_part(0, 1)
                s_part(0)
                pT_part(1)
                theta_part(0)
                t1_part(0)
                x1_part(1, 0)
                s_part(1)
                x1_part(1, 1)
                if not last:
                    t1_part(1)
                    act.wait_ge(gphi_done, four[4])
                    c_part(0, loads[32])
                    tT_part(0, four[5])
                    c_part(1, loads[32])
                    tT_part(1, four[6])
                    theta_part(1)
                    tT_part(2, four[7])
                    tT_part(3, four[8])
                else:
                    t1_part(1)
                    theta_part(1)

            pair(0, first=True)
            with act.Fori(1, PAIRS - 1) as p:
                pair(p)
            pair(PAIRS - 1, last=True)

        @block.vector
        def _(dve):
            def lo(parts, hi_made, count, at, src, made):
                dve.wait_ge(hi_made, count)
                dve.tensor_tensor(parts[1][at], src, parts[0][at].bitcast(F32), ALU.subtract).then_inc(made, 1)

            every = slice(None)
            for n in range(2 * KH):
                at = (every, n % KH)
                (lhs_raw, lhs), (rhs_raw, rhs) = ((wk_raw, wk), (wq_raw, wq)) if n < KH else ((wv_raw, wv), (wo_raw, wo))
                dve.wait_ge(w_loaded[n], 32)
                dve.tensor_copy(rhs[0][at], rhs_raw[at]).then_inc(rhs_hi, 1)
                lo(lhs, lhs_hi, n + 1, at, lhs_raw[at], w_lo)
                lo(rhs, rhs_hi, n + 1, at, rhs_raw[at], w_lo)

            def cT_parts(reached):
                for half in range(2):
                    at = (every, slice(2 * half, 2 * half + 2))
                    lo(cT, cT_hi, reached[half], at, cT_raw[at], cT_lo)

            def xT_part(b, count):
                lo(xT, xT_hi, count, (every, b), xT_raw[:, b], xT_lo)

            def c_part(b, count):
                lo(cn, c_hi, count, (every, b), c_raw[:, b], c_lo)

            def tT_part(m, count):
                lo(tT, tT_hi, count, (every, m), bank[TT_BANK[m]][:].rearrange("p (b s) -> p b s", b=2), tT_lo)

            dve.wait_ge(params_loaded, 32)
            dve.tensor_scalar(bn_row[:], row[:, ROW_VAR:ROW_VAR + L], EPS, None, ALU.add).then_inc(var_made, 1)
            dve.tensor_scalar(bn_col[:], col[:, VAR:VAR + KL], EPS, None, ALU.add).then_inc(var_made, 1)
            for m in range(KH):
                lo(qk, qk_hi, m + 1, (every, m), bank[m][:], qk_lo)
            cT_parts([1, 2])
            lo(gphi_w, small_hi, 1, (every,), gphi_raw[:], small_lo)
            lo(theta_w, small_hi, 2, (every,), theta_raw[:], small_lo)
            dve.wait_ge(std_made, 2)
            dve.reciprocal(bn_row[:], std_row[:]).then_inc(bn_step, 1)
            dve.reciprocal(bn_col[:], std_col[:]).then_inc(bn_step, 1)
            dve.wait_ge(bn_step, 2)
            dve.scalar_tensor_tensor(out=bn_row[:], in0=bn_row[:], scalar=1.0 / H, in1=row[:, ROW_GAMMA:ROW_GAMMA + L],
                                     op0=ALU.mult, op1=ALU.mult).then_inc(bn_step, 1)
            dve.tensor_tensor(bn_col[:], bn_col[:], col[:, GAMMA:GAMMA + KL], ALU.mult).then_inc(bn_step, 1)
            dve.tensor_tensor(out_bias[:], col[:, W_B:W_B + KL], col[:, MEAN:MEAN + KL], ALU.subtract).then_inc(bn_step, 1)
            dve.wait_ge(bn_step, 5)
            dve.tensor_tensor(ww_raw[:], ww_raw[:], bn_row[:], ALU.mult).then_inc(ww_scaled, 1)
            dve.tensor_tensor(out_bias[:], out_bias[:], bn_col[:], ALU.mult).then_inc(bn_step, 1)
            dve.wait_ge(bn_step, 6)
            dve.tensor_tensor(out_bias[:], out_bias[:], col[:, BETA:BETA + KL], ALU.add).then_inc(bn_step, 1)
            dve.wait_ge(bn_step, 7)
            for m in range(KH):
                dve.wait_ge(ov_hi, m + 1)
                dve.scalar_tensor_tensor(out=ov[1][:, m, :], in0=bank[KH + m][:], scalar=row[:, ROW_ALPHA:ROW_ALPHA + 1],
                                         in1=ov[0][:, m, :].bitcast(F32), op0=ALU.mult,
                                         op1=ALU.subtract).then_inc(ov_lo, 1)
            for b in range(2):
                xT_part(b, b + 1)
            for n, m in enumerate(FIRST_T[:-1]):
                tT_part(m, n + 1)
            tT_part(FIRST_T[-1], KH)
            c_part(0, 1)
            c_part(1, 2)
            lo(ww, ww_hi, 1, (every,), ww_raw[:], ww_lo)

            def pair(p, last=False):
                loads = counts(dve, p, 16, [16])
                two, four = counts(dve, p, 2, range(1, 5)), counts(dve, p, 4, range(1, 9))

                def row_maxima(b):
                    dve.wait_ge(scores_done, two[b + 1])
                    dve.tensor_reduce(row_max[:, b], bank[SCORE_BANK[b]][:].rearrange("p (t s) -> p t s", t=KL),
                                      AX.X, ALU.max).then_inc(max_made, 1)
                    dve.wait_ge(max_made, two[b + 1])
                    dve.tensor_scalar(neg_max[:, b], row_max[:, b], -SCALE, None, ALU.mult).then_inc(neg_max_made, 1)

                def invert_sums(b):
                    dve.wait_ge(probs_made, two[b + 1])
                    dve.reciprocal(inv_sum[:, b], row_sum[:, b]).then_inc(inv_sum_made, 1)

                def vo_parts(b):
                    for st in range(KS):
                        lo(vo, vo_hi, four[2 * b + st + 1], (every, b, st), bank[VO_BANK[b][st]][:], vo_lo)

                def pT_part(b):
                    lo(pT, pT_hi, two[b + 1], (every, b),
                       bank[PT_BANK[b]][:].rearrange("p (t l) -> p t l", t=KS), pT_lo)

                def gphi_rows(b):
                    for half in range(2):
                        dve.wait_ge(gphi_done, four[2 * b + half + 1])
                        for j in range(2):
                            g = dve.tensor_tensor(gphi[:, 2 * half + j], bank[GPHI_BANK[b][half]][:, j * 2 * CI:(j + 1) * 2 * CI],
                                                  row[:, ROW_GPHI_B:ROW_GPHI_B + 2 * CI], ALU.add)
                        g.then_inc(gphi_made, 1)

                def x1_rows(b):
                    dve.wait_ge(x_loaded[b], loads[16])
                    dve.wait_ge(inv_sum_made, two[b + 1])
                    for lt in range(KL):
                        dve.wait_ge(delta_done, four[2 * b + lt + 1])
                        dve.scalar_tensor_tensor(out=xb[:, b, lt], in0=bank[DELTA_BANK[b][lt]][:],
                                                 scalar=inv_sum[:, b, lt:lt + 1], in1=xb[:, b, lt],
                                                 op0=ALU.mult, op1=ALU.add).then_inc(x1_made, 1)

                def x1_part(b, lt):
                    lo(x1, x1_hi, four[2 * b + lt + 1], (every, b, lt), xb[:, b, lt], x1_lo)

                def s_part(b):
                    lo(s, s_hi, two[b + 1], (every,), bank[S_BANK[b]][:, 0:CI], s_lo)

                def t1_part(b):
                    lo(t1, t1_hi, two[b + 1], (every, b), bank[T1_BANK[b]][:, 0:L], t1_lo)

                def theta_part(b):
                    dve.wait_ge(theta_hi, two[b + 1])
                    dve.scalar_tensor_tensor(out=theta[1][:, b], in0=bank[THETA_BANK[b]][:],
                                             scalar=col[:, THETA_B:THETA_B + 1], in1=theta[0][:, b].bitcast(F32),
                                             op0=ALU.add, op1=ALU.subtract).then_inc(theta_lo, 1)

                def out_rows(b, ct):
                    banks = (LAST_OUT_BANK if last else OUT_BANK)[b]
                    dve.wait_ge(out_done, four[2 * b + ct + 1])
                    dve.scalar_tensor_tensor(out=xb[:, b, ct], in0=bank[banks[ct]][:],
                                             scalar=out_bias[:, ct:ct + 1], in1=xb[:, b, ct],
                                             op0=ALU.add, op1=ALU.add).then_inc(out_made, 1)

                row_maxima(0)
                row_maxima(1)
                if not last:
                    for b in range(2):
                        xT_part(b, two[b + 3])
                invert_sums(0)
                vo_parts(0)
                invert_sums(1)
                pT_part(0)
                vo_parts(1)
                if not last:
                    cT_parts([two[3], two[4]])
                gphi_rows(0)
                x1_rows(0)
                x1_part(0, 0)
                x1_part(0, 1)
                s_part(0)
                pT_part(1)
                gphi_rows(1)
                theta_part(0)
                t1_part(0)
                x1_rows(1)
                x1_part(1, 0)
                s_part(1)
                x1_part(1, 1)
                out_rows(0, 0)
                t1_part(1)
                out_rows(0, 1)
                if not last:
                    tT_part(0, four[5])
                    c_part(0, two[3])
                    tT_part(1, four[6])
                    c_part(1, two[4])
                theta_part(1)
                if not last:
                    tT_part(2, four[7])
                    tT_part(3, four[8])
                out_rows(1, 0)
                out_rows(1, 1)

            pair(0)
            with dve.Fori(1, PAIRS - 1) as p:
                pair(p)
            pair(PAIRS - 1, last=True)

        @block.gpsimd
        def _(pool):
            pool.memset(idle[:], 0.0).then_inc(idle_zeroed, 1)
            pool.memset(ident[:], 0.0).then_inc(ident_zeroed, 1)
            pool.wait_ge(ident_zeroed, 1)
            pool.affine_select(out=ident[:], in_=ident[:], compare_op=ALU.not_equal, fill=1.0, base=0,
                               pattern=[[-1, P]], channel_multiplier=1).then_inc(ident_made, 1)


def kernel(**inputs):
    import concourse.bacc as bacc
    from concourse.bass_utils import run_bass_kernel_spmd

    a = {n: np.asarray(v) for n, v in inputs.items()}

    def pairs(t, rows_of):
        t = t.reshape(PAIRS, 2, rows_of, P, t.shape[-1])
        return t.transpose(0, 3, 1, 2, 4)

    x, ctx = a["x"], a["ctx_2048"]
    l1 = "L1_xattn_"
    per_channel = [a[l1 + n].reshape(KL, P).T for n in ("w_b", "bn_gamma", "bn_beta", "bn_mean", "bn_var")]
    arrays = {
        "x": pairs(x, KL),
        "x_t": pairs(x.transpose(0, 2, 1), KH),
        "ctx_n": pairs(ctx, KS),
        "ctx_t": pairs(ctx.transpose(0, 2, 1), KH).transpose(0, 1, 3, 2, 4),
        "w_q": a["L0_xattn_w_q"],
        "w_k": a["L0_xattn_w_k"],
        "w_v": a["L0_xattn_w_v"],
        "w_o_t": a["L0_xattn_w_o"].T,
        "gphi_w_t": np.concatenate([a[l1 + "g_w"], a[l1 + "phi_w"]]).T,
        "theta_w_t": a[l1 + "theta_w"].T,
        "w_w_t": a[l1 + "w_w"].T,
        "cols": np.concatenate(per_channel + [a[l1 + "theta_b"].reshape(CI, 1)], axis=1),
        "rows": np.concatenate([a[l1 + "g_b"], a[l1 + "phi_b"], a[l1 + "bn_gamma"], a[l1 + "bn_var"],
                                a["L0_xattn_alpha"].reshape(1)]),
    }
    arrays = {n: np.ascontiguousarray(v) for n, v in arrays.items()}
    nc = bacc.Bacc("TRN2", target_bir_lowering=False, num_devices=1)
    args = {n: nc.dram_tensor(n, v.shape, F32, kind="ExternalInput").ap() for n, v in arrays.items()}
    out = nc.dram_tensor("out", (PAIRS, P, 2, KL, H), F32, kind="ExternalOutput").ap()
    two_stage_cross_attention(nc, out=out, **args)
    got = run_bass_kernel_spmd(nc, [arrays], core_ids=[0]).results[0]["out"]
    return got.transpose(0, 2, 3, 1, 4).reshape(B, L, H)
```
